# Optimizing a Trainium2 kernel written in Bass

```python
import numpy as np
import jax
import jax.numpy as jnp

def _softmax(x, axis=-1):
    return jax.nn.softmax(x, axis=axis)

def _gelu(x):
    return jax.nn.gelu(x, approximate=True)

def _silu(x):
    return jax.nn.silu(x)

def _sigmoid(x):
    return jax.nn.sigmoid(x)

def _layernorm(x, axis=-1, eps=1e-05):
    m = jnp.mean(x, axis=axis, keepdims=True)
    v = jnp.var(x, axis=axis, keepdims=True)
    return (x - m) / jnp.sqrt(v + eps)

def _scatter_add(tgt, idx, src, axis=0):
    return tgt.at[idx].add(src)

def _segment_sum(src, seg, n):
    return jax.ops.segment_sum(src, seg, n)
kernel_name = 'mk_gnn_resnorm_d4_gnn_r8_a2dda4'

def setup_inputs(seed: int=0):
    np.random.seed(seed)
    _w = jnp.asarray

    def _rec_inputs():
        import jax
        import jax.numpy as jnp
        _gk = jax.random.key(seed)
        x = -0.0005121 + 1.001 * jax.random.normal(jax.random.fold_in(_gk, 1), (6250, 64), jnp.float32)
        src = jax.random.randint(jax.random.fold_in(_gk, 2), (200000,), 0, 6250, jnp.int32)
        dst = jnp.minimum((6250 * jax.random.uniform(jax.random.fold_in(_gk, 3), (200000,)) ** 2.0).astype(jnp.int32), 49999)
        _o = jnp.argsort(dst, stable=True)
        src = src[_o]
        dst = dst[_o]
        edge_attr_32 = 0.000196303 + 1.00016 * jax.random.normal(jax.random.fold_in(_gk, 12), (200000, 32), jnp.float32)
        edge_type_8 = jax.random.randint(jax.random.fold_in(_gk, 14), (200000,), 0, 8, jnp.int32)
        return (x, src, dst, edge_attr_32, edge_type_8)
    x, src, dst, edge_attr_32, edge_type_8 = _rec_inputs()

    def _L0_gnn_setup():
        import jax, jax.numpy as jnp
        import numpy as np
        N_NODES = 6250
        N_EDGES = 100000
        FEAT_DIM = 64
        NUM_RELS = 8
        key = jax.random.key(seed)
        k1, k2, k3, k4, k5 = jax.random.split(key, 5)
        features = jax.random.normal(k1, (N_NODES, FEAT_DIM), dtype=jnp.float32)
        limit = np.sqrt(2.0) * np.sqrt(6.0 / (FEAT_DIM + FEAT_DIM))
        weight_r = jax.random.uniform(k2, (NUM_RELS, FEAT_DIM, FEAT_DIM), dtype=jnp.float32, minval=-limit, maxval=limit)
        src = jax.random.randint(k3, (N_EDGES,), 0, N_NODES, dtype=jnp.int64 if jax.config.jax_enable_x64 else jnp.int32)
        dst = jax.random.randint(k4, (N_EDGES,), 0, N_NODES, dtype=src.dtype)
        etype = jax.random.randint(k5, (N_EDGES,), 0, NUM_RELS, dtype=src.dtype)
        return {'features': features, 'weight_r': weight_r, 'src': src, 'dst': dst, 'etype': etype}
    _L0_gnn_all = _L0_gnn_setup()
    _L0_gnn_in = {k: v for k, v in _L0_gnn_all.items() if k in ('weight_r',)}
    del _L0_gnn_all

    def _L1_gnn_setup():
        import jax, jax.numpy as jnp
        import numpy as np
        N, E, H, ED = (6250, 100000, 64, 32)

        def _layernorm(h, gamma, beta, eps=1e-05):
            mu = jnp.mean(h, axis=-1, keepdims=True)
            var = jnp.mean(jnp.square(h - mu), axis=-1, keepdims=True)
            return (h - mu) * jax.lax.rsqrt(var + eps) * gamma + beta
        key = jax.random.key(seed)
        ks = jax.random.split(key, 16)
        s = lambda fan_in: 1.0 / np.sqrt(fan_in)
        inp = {'x': jax.random.normal(ks[0], (N, H), dtype=jnp.float32), 'edge_index': jax.random.randint(ks[1], (2, E), 0, N, dtype=jnp.int64), 'edge_attr': jax.random.normal(ks[2], (E, ED), dtype=jnp.float32), 'w1': jax.random.uniform(ks[3], (2 * H + ED, H), jnp.float32, -s(2 * H + ED), s(2 * H + ED)), 'b1': jnp.zeros((H,), jnp.float32), 'w2': jax.random.uniform(ks[4], (H, H), jnp.float32, -s(H), s(H)), 'b2': jnp.zeros((H,), jnp.float32), 'w3': jax.random.uniform(ks[5], (2 * H, H), jnp.float32, -s(2 * H), s(2 * H)), 'b3': jnp.zeros((H,), jnp.float32), 'w4': jax.random.uniform(ks[6], (H, H), jnp.float32, -s(H), s(H)), 'b4': jnp.zeros((H,), jnp.float32), 'gamma': jnp.ones((H,), jnp.float32), 'beta': jnp.zeros((H,), jnp.float32)}
        return inp
    _L1_gnn_all = _L1_gnn_setup()
    _L1_gnn_in = {k: v for k, v in _L1_gnn_all.items() if k in ('w1', 'b1', 'w2', 'b2', 'w3', 'b3', 'w4', 'b4', 'gamma', 'beta')}
    del _L1_gnn_all

    def _L2_gnn_setup():
        import jax, jax.numpy as jnp
        import numpy as np
        N_NODES = 6250
        N_EDGES = 100000
        D = 64
        NEG_SLOPE = 0.2

        def _gat_conv(x, src, dst, W, a_src, a_dst, b, n_nodes):
            h = x @ W
            alpha_s = h @ a_src
            alpha_d = h @ a_dst
            e = alpha_s[src] + alpha_d[dst]
            e = jnp.where(e > 0, e, NEG_SLOPE * e)
            m = jax.ops.segment_max(e, dst, num_segments=n_nodes)
            m = jnp.where(jnp.isfinite(m), m, 0.0)
            ex = jnp.exp(e - m[dst])
            s = jax.ops.segment_sum(ex, dst, num_segments=n_nodes)
            alpha = ex / (s[dst] + 1e-16)
            out = jax.ops.segment_sum(alpha[:, None] * h[src], dst, num_segments=n_nodes)
            return out + b

        def _add_self_loops(edge_index, n_nodes):
            loop = jnp.arange(n_nodes, dtype=edge_index.dtype)
            src = jnp.concatenate([edge_index[0], loop])
            dst = jnp.concatenate([edge_index[1], loop])
            return (src, dst)
        key = jax.random.key(seed)
        ks = jax.random.split(key, 16)
        x = jax.random.normal(ks[0], (N_NODES, D), dtype=jnp.float32)
        edge_index = jax.random.randint(ks[1], (2, N_EDGES), 0, N_NODES, dtype=jnp.int32)
        sc = 1.0 / np.sqrt(D)

        def lin(k):
            return jax.random.uniform(k, (D, D), jnp.float32, -sc, sc)

        def att(k):
            return jax.random.uniform(k, (D,), jnp.float32, -sc, sc)
        return {'x': x, 'edge_index': edge_index, 'W1': lin(ks[2]), 'a1s': att(ks[3]), 'a1d': att(ks[4]), 'b1': jnp.zeros((D,), jnp.float32), 'W2': lin(ks[5]), 'a2s': att(ks[6]), 'a2d': att(ks[7]), 'b2': jnp.zeros((D,), jnp.float32), 'W3': lin(ks[8]), 'a3s': att(ks[9]), 'a3d': att(ks[10]), 'b3': jnp.zeros((D,), jnp.float32)}
    _L2_gnn_all = _L2_gnn_setup()
    _L2_gnn_in = {k: v for k, v in _L2_gnn_all.items() if k in ('W1', 'a1s', 'a1d', 'b1', 'W2', 'a2s', 'a2d', 'b2', 'W3', 'a3s', 'a3d', 'b3')}
    del _L2_gnn_all

    def _L3_gnn_setup():
        import jax, jax.numpy as jnp
        import numpy as np
        N_NODES = 8192
        N_EDGES = 131072
        DIM = 64
        K_HOPS = 3
        ALPHA = 0.1
        key = jax.random.key(seed)
        k1, k2, k3, k4 = jax.random.split(key, 4)
        features = jax.random.normal(k1, (N_NODES, DIM), dtype=jnp.float32)
        src = jax.random.randint(k2, (N_EDGES,), 0, N_NODES, dtype=jnp.int32)
        dst = jax.random.randint(k3, (N_EDGES,), 0, N_NODES, dtype=jnp.int32)
        attn_w = jax.random.normal(k4, (2 * DIM,), dtype=jnp.float32) * 0.1
        attn_b = jnp.zeros((1,), dtype=jnp.float32)
        temp = np.asarray(ALPHA * (1 - ALPHA) ** np.arange(K_HOPS + 1), dtype=np.float32)
        temp[-1] = (1 - ALPHA) ** K_HOPS
        temp = jnp.asarray(temp)
        return {'features': features, 'src': src, 'dst': dst, 'attn_w': attn_w, 'attn_b': attn_b, 'temp': temp}
    _L3_gnn_all = _L3_gnn_setup()
    _L3_gnn_in = {k: v for k, v in _L3_gnn_all.items() if k in ('attn_w', 'attn_b', 'temp')}
    del _L3_gnn_all
    return {'x': x, 'src': src, 'dst': dst, 'edge_attr_32': edge_attr_32, 'edge_type_8': edge_type_8, 'L0_gnn_weight_r': _L0_gnn_in['weight_r'], 'L1_gnn_w1': _L1_gnn_in['w1'], 'L1_gnn_b1': _L1_gnn_in['b1'], 'L1_gnn_w2': _L1_gnn_in['w2'], 'L1_gnn_b2': _L1_gnn_in['b2'], 'L1_gnn_w3': _L1_gnn_in['w3'], 'L1_gnn_b3': _L1_gnn_in['b3'], 'L1_gnn_w4': _L1_gnn_in['w4'], 'L1_gnn_b4': _L1_gnn_in['b4'], 'L1_gnn_gamma': _L1_gnn_in['gamma'], 'L1_gnn_beta': _L1_gnn_in['beta'], 'L2_gnn_W1': _L2_gnn_in['W1'], 'L2_gnn_a1s': _L2_gnn_in['a1s'], 'L2_gnn_a1d': _L2_gnn_in['a1d'], 'L2_gnn_b1': _L2_gnn_in['b1'], 'L2_gnn_W2': _L2_gnn_in['W2'], 'L2_gnn_a2s': _L2_gnn_in['a2s'], 'L2_gnn_a2d': _L2_gnn_in['a2d'], 'L2_gnn_b2': _L2_gnn_in['b2'], 'L2_gnn_W3': _L2_gnn_in['W3'], 'L2_gnn_a3s': _L2_gnn_in['a3s'], 'L2_gnn_a3d': _L2_gnn_in['a3d'], 'L2_gnn_b3': _L2_gnn_in['b3'], 'L3_gnn_attn_w': _L3_gnn_in['attn_w'], 'L3_gnn_attn_b': _L3_gnn_in['attn_b'], 'L3_gnn_temp': _L3_gnn_in['temp']}

def reference(x, src, dst, edge_attr_32, edge_type_8, L0_gnn_weight_r, L1_gnn_w1, L1_gnn_b1, L1_gnn_w2, L1_gnn_b2, L1_gnn_w3, L1_gnn_b3, L1_gnn_w4, L1_gnn_b4, L1_gnn_gamma, L1_gnn_beta, L2_gnn_W1, L2_gnn_a1s, L2_gnn_a1d, L2_gnn_b1, L2_gnn_W2, L2_gnn_a2s, L2_gnn_a2d, L2_gnn_b2, L2_gnn_W3, L2_gnn_a3s, L2_gnn_a3d, L2_gnn_b3, L3_gnn_attn_w, L3_gnn_attn_b, L3_gnn_temp):
    import jax
    import jax.numpy as jnp

    def _L0_gnn_ref(features, weight_r, src, dst, etype):
        import jax, jax.numpy as jnp
        import numpy as np
        N_NODES = 6250
        N_EDGES = 100000
        FEAT_DIM = 64
        NUM_RELS = 8
        N, D = features.shape
        c = 0.2
        deg = jax.ops.segment_sum(jnp.ones(dst.shape, dtype=features.dtype), dst, num_segments=N)
        hw = jnp.einsum('nd,rdf->rnf', features, weight_r)
        msg = hw[etype, src] / deg[dst][:, None]
        M = jax.ops.segment_sum(msg, dst, num_segments=N)
        updated = jax.nn.relu(c * features + (1.0 - c) * M)
        return jnp.where((deg > 0)[:, None], updated, features)

    def _L1_gnn_ref(x, edge_index, edge_attr, w1, b1, w2, b2, w3, b3, w4, b4, gamma, beta):
        import jax, jax.numpy as jnp
        import numpy as np
        N, E, H, ED = (6250, 100000, 64, 32)

        def _layernorm(h, gamma, beta, eps=1e-05):
            mu = jnp.mean(h, axis=-1, keepdims=True)
            var = jnp.mean(jnp.square(h - mu), axis=-1, keepdims=True)
            return (h - mu) * jax.lax.rsqrt(var + eps) * gamma + beta
        source, target = (edge_index[0], edge_index[1])
        m_in = jnp.concatenate([x[source], x[target], edge_attr], axis=-1)
        m = jax.nn.silu(m_in @ w1 + b1) @ w2 + b2
        agg = jax.ops.segment_sum(m, target, num_segments=x.shape[0])
        u_in = jnp.concatenate([x, agg], axis=-1)
        upd = jax.nn.silu(u_in @ w3 + b3) @ w4 + b4
        return _layernorm(x + upd, gamma, beta)

    def _L2_gnn_ref(x, edge_index, W1, a1s, a1d, b1, W2, a2s, a2d, b2, W3, a3s, a3d, b3):
        import jax, jax.numpy as jnp
        import numpy as np
        N_NODES = 6250
        N_EDGES = 100000
        D = 64
        NEG_SLOPE = 0.2

        def _gat_conv(x, src, dst, W, a_src, a_dst, b, n_nodes):
            h = x @ W
            alpha_s = h @ a_src
            alpha_d = h @ a_dst
            e = alpha_s[src] + alpha_d[dst]
            e = jnp.where(e > 0, e, NEG_SLOPE * e)
            m = jax.ops.segment_max(e, dst, num_segments=n_nodes)
            m = jnp.where(jnp.isfinite(m), m, 0.0)
            ex = jnp.exp(e - m[dst])
            s = jax.ops.segment_sum(ex, dst, num_segments=n_nodes)
            alpha = ex / (s[dst] + 1e-16)
            out = jax.ops.segment_sum(alpha[:, None] * h[src], dst, num_segments=n_nodes)
            return out + b

        def _add_self_loops(edge_index, n_nodes):
            loop = jnp.arange(n_nodes, dtype=edge_index.dtype)
            src = jnp.concatenate([edge_index[0], loop])
            dst = jnp.concatenate([edge_index[1], loop])
            return (src, dst)
        n = x.shape[0]
        src, dst = _add_self_loops(edge_index, n)
        h = _gat_conv(x, src, dst, W1, a1s, a1d, b1, n)
        h = jax.nn.relu(h)
        h = _gat_conv(h, src, dst, W2, a2s, a2d, b2, n)
        h = jax.nn.relu(h)
        return _gat_conv(h, src, dst, W3, a3s, a3d, b3, n)

    def _L3_gnn_ref(features, src, dst, attn_w, attn_b, temp):
        import jax, jax.numpy as jnp
        import numpy as np
        N_NODES = 8192
        N_EDGES = 131072
        DIM = 64
        K_HOPS = 3
        ALPHA = 0.1
        N, D = features.shape
        a_src, a_dst = (attn_w[:D], attn_w[D:])
        out = features * temp[0]
        feats = features
        n_hops = temp.shape[0] - 1
        for k in range(n_hops):
            z_src = feats[src]
            e = jax.nn.leaky_relu(z_src @ a_src + feats[dst] @ a_dst + attn_b)
            m = jax.ops.segment_max(e, dst, num_segments=N)
            ex = jnp.exp(e - m[dst])
            denom = jax.ops.segment_sum(ex, dst, num_segments=N)
            w = ex / denom[dst]
            feats = jax.ops.segment_sum(z_src * w[:, None], dst, num_segments=N)
            out = out + temp[k + 1] * feats
        return out
    edge_index = jnp.stack([src, dst])
    x = _layernorm(x + _L0_gnn_ref(x, L0_gnn_weight_r, src, dst, edge_type_8), axis=-1)
    x = _layernorm(x + _L1_gnn_ref(x, edge_index, edge_attr_32, L1_gnn_w1, L1_gnn_b1, L1_gnn_w2, L1_gnn_b2, L1_gnn_w3, L1_gnn_b3, L1_gnn_w4, L1_gnn_b4, L1_gnn_gamma, L1_gnn_beta), axis=-1)
    x = _layernorm(x + _L2_gnn_ref(x, edge_index, L2_gnn_W1, L2_gnn_a1s, L2_gnn_a1d, L2_gnn_b1, L2_gnn_W2, L2_gnn_a2s, L2_gnn_a2d, L2_gnn_b2, L2_gnn_W3, L2_gnn_a3s, L2_gnn_a3d, L2_gnn_b3), axis=-1)
    x = _layernorm(x + _L3_gnn_ref(x, src, dst, L3_gnn_attn_w, L3_gnn_attn_b, L3_gnn_temp), axis=-1)
    return x

_drawn_inputs = setup_inputs


def setup_inputs(seed=0):
    import zlib

    import numpy as np

    out = dict(_drawn_inputs(seed))
    spreads = {'L1_gnn_b1': (0.0, 0.1),
     'L1_gnn_b2': (0.0, 0.1),
     'L1_gnn_b3': (0.0, 0.315),
     'L1_gnn_b4': (0.0, 0.1),
     'L1_gnn_gamma': (1.0, 0.2),
     'L1_gnn_beta': (0.0, 0.1),
     'L2_gnn_b1': (0.0, 0.383),
     'L2_gnn_b2': (0.0, 0.1),
     'L2_gnn_b3': (0.0, 0.1)}
    factors = {'L2_gnn_a1s': 8.0,
     'L2_gnn_a1d': 64.0,
     'L2_gnn_a2s': 38.823,
     'L2_gnn_a2d': 64.0,
     'L2_gnn_a3s': 64.0,
     'L2_gnn_a3d': 64.0}
    for name, (base, spread) in spreads.items():
        noise = np.random.default_rng([zlib.crc32(name.encode()), seed]).standard_normal(out[name].shape)
        drawn = base * np.exp(spread * noise) if base else spread * noise
        out[name] = jnp.asarray(drawn.astype(out[name].dtype))
    for name, factor in factors.items():
        out[name] = (out[name] * factor).astype(out[name].dtype)
    return out
```

```python
from contextlib import ExitStack

import concourse.bass as bass
from concourse import mybir

ALU = mybir.AluOpType
ACT = mybir.ActivationFunctionType
AX_X = mybir.AxisListType.X
F32 = mybir.dt.float32
BF16 = mybir.dt.bfloat16
I32 = mybir.dt.int32
U32 = mybir.dt.uint32

P = 128
H = 64
W = H + 2
TILES = 4
GROUP = TILES * P
RING = 4
BIG = float(2.0 ** 100)
EPS_LN = 1e-5


def gnn_kernel(nc, x_in, src_in, dst_in, ea_in, et_in, w_rel, w1, b1, w2, b2, w3, b3, w4, b4,
               gamma, beta, gat, attn_w, attn_b, temp, out):
    N = x_in.shape[0]
    E, ED = ea_in.shape
    RELS = w_rel.shape[0]
    BLOCKS = -(-N // P)
    NB = -(-BLOCKS // 4) * 4
    NP = NB * P
    EP = max(p for p in range(1, P + 1) if E % p == 0)
    EC = E // EP
    NG = -(-((E + BLOCKS * (GROUP - 1)) // GROUP) // RING) * RING
    ITERS = NG // RING
    REC = 4 + ED
    CH = 25
    assert EC % (2 * CH) == 0 and E < 2 ** 24 and RELS * NP < 2 ** 24

    rec = nc.dram_tensor("placed_edges", (NG * GROUP, REC), F32, kind="Internal").ap()
    table = nc.dram_tensor("node_table", (NP, W), F32, kind="Internal").ap()
    hw_table = nc.dram_tensor("relation_table", (RELS * NP, W), F32, kind="Internal").ap()
    rec_groups = rec.rearrange("(g p j) w -> g p (j w)", p=P, j=TILES)
    table_blocks = table.rearrange("(b p) w -> p b w", p=P)
    hw_blocks = hw_table.rearrange("(r b p) w -> b p r w", r=RELS, p=P)
    src_e = src_in.rearrange("(p c) -> p c", p=EP)
    dst_e = dst_in.rearrange("(p c) -> p c", p=EP)
    et_e = et_in.rearrange("(p c) -> p c", p=EP)
    ea_e = ea_in.rearrange("(p c) d -> p c d", p=EP)

    def row(vec):
        return vec.rearrange("(a d) -> a d", a=1)

    base = {}

    def wait(eng, sem, more):
        if isinstance(more, int) and more <= 0:
            return
        eng.wait_ge(sem, more + base[sem.name])

    def hold(eng, sem, more):
        if isinstance(more, int) and more <= 0:
            return
        eng.wait_ge(sem, more + base[sem.name])
        eng.sem_inc(passed, 1)

    def grown(sem, by):
        base[sem.name] += by

    with ExitStack() as top:
        def sb(name, shape, dt=F32, ctx=top):
            return ctx.enter_context(nc.sbuf_tensor(name, shape, dt))

        def sem(name):
            s = top.enter_context(nc.semaphore(name))
            base[s.name] = 0
            return s

        x = sb("x", [P, NB, H])
        acc = sb("acc", [P, NB, W])
        tab = sb("tab", [P, NB, W])
        aux = sb("aux", [P, NB, H])
        state = sb("state", [P, NB, 2])
        deg = sb("deg", [P, NB])
        src_slot = sb("src_slot", [P, (NG + 2) * TILES])
        hwr_slot = sb("hwr_slot", [P, (NG + 2) * TILES])
        dst_slot = sb("dst_slot", [P, NG * TILES])
        dst_slot16 = sb("dst_slot16", [P, (NG + 2) * TILES], BF16)
        block_of = sb("block_of", [1, NG], I32)
        ident = sb("ident", [P, P])
        ident16 = sb("ident16", [P, P], BF16)
        iota_row = sb("iota_row", [P, P])
        iota_col = sb("iota_col", [P, 1])
        ones = sb("ones", [P, P])

        psum = [top.enter_context(nc.psum_tensor(f"ps{i}", [P, 512], F32)) for i in range(8)]

        go = sem("constants_ready")
        passed = sem("waits_passed")
        chain = sem("chain")
        s_in = sem("inputs_loaded")
        s_out = sem("stores_done")
        s_tab = sem("table_stored")
        idx_staged = sem("idx_staged")
        gathered = [sem(f"gathered{u}") for u in range(RING)]
        loaded = [sem(f"loaded{u}") for u in range(RING)]
        s_dst = sem("dst_staged")
        s_row = sem("row_done")
        s_mask = sem("mask_done")
        s_hot_t = sem("onehot_t_done")
        s_as = sem("score_rows_done")
        s_old = sem("old_state_staged")
        s_max = sem("max_done")
        s_upd = sem("state_updated")
        s_sum = sem("pair_summed")
        s_mu = sem("shift_done")
        s_decay = sem("decay_done")
        s_ed = sem("edge_target_done")
        s_z = sem("edge_z_done")
        s_l = sem("edge_lrelu_done")
        s_x = sem("edge_exponent_done")
        s_w = sem("edge_weight_done")
        s_hot = sem("onehot_done")
        s_scat = sem("scattered")
        s_acc = sem("accumulated")

        chain_end = [0]
        with ExitStack() as ph:
            def t(name, shape, dt=F32):
                return sb(name, shape, dt, ph)

            dst_i = t("dst_i", [EP, EC], I32)
            src_i = t("src_i", [EP, EC], I32)
            et_i = t("et_i", [EP, EC], I32)
            blk = t("blk", [EP, EC])
            loc = t("loc", [EP, EC])
            srcf = t("srcf", [EP, EC])
            hwr = t("hwr", [EP, EC])
            eq = t("eq", [EP, EC])
            eq_i = t("eq_i", [EP, EC], I32)
            cum = t("cum", [EP, EC])
            tmp = t("tmp", [EP, EC])
            pos = t("pos", [EP, EC])
            kcol = t("kcol", [P, BLOCKS])
            cnt = t("cnt", [EP, BLOCKS])
            tri = t("tri", [P, P])
            toti = t("toti", [P, BLOCKS], I32)
            ng = t("ng", [P, BLOCKS])
            endg = t("endg", [P, BLOCKS])
            basep = t("basep", [P, BLOCKS])
            grow = t("grow", [1, NG])
            ge = t("ge", [1, NG // 4, BLOCKS], BF16)
            gbf = t("gbf", [1, NG])
            blank = t("blank", [P, TILES, REC])
            reci = t("reci", [EP, 2, CH, REC])
            eas = t("eas", [EP, 2, CH * ED])
            posi = t("posi", [EP, 2, CH], U32)
            meta = t("meta", [P, 2, 8, TILES * REC])
            s_blank = sem("blanks_stored")
            s_eq = sem("eq_done")
            s_cum = sem("cum_done")
            s_prod = sem("product_done")
            s_rank = sem("rank_added")
            s_rec = sem("records_built")
            s_ea = [sem(f"attributes_loaded{u}") for u in range(2)]
            s_placed = [sem(f"placed{u}") for u in range(2)]
            s_meta = sem("slots_copied")
            s_cnt = sem("counts_done")
            s_pre = sem("prefix_done")
            s_pos = sem("positions_done")
            block = ph.enter_context(nc.Block())

            @block.sync
            def _(sp):
                sp.dma_start(dst_i[:, :], dst_e).then_inc(s_in, 16)
                sp.dma_start(src_i[:, :], src_e).then_inc(s_in, 16)
                sp.dma_start(et_i[:, :], et_e).then_inc(s_in, 16)
                full = N // P
                sp.wait_ge(go, 1)
                sp.dma_start(x[:, 0:full, :], x_in[0:full * P, :].rearrange("(b p) f -> p b f", p=P)).then_inc(s_in, 16)
                if N % P:
                    sp.dma_start(x[0:N % P, full, :], x_in[full * P:N, :]).then_inc(s_in, 16)
                for g in range(0, NG, 8):
                    sp.dma_start(rec_groups[g:g + 8].rearrange("g p w -> p g w"),
                                 blank[:, :, :].rearrange("p j w -> p (j w)").unsqueeze(1).to_broadcast([P, 8, TILES * REC])).then_inc(s_blank, 16)
                def load(i):
                    for u in range(2):
                        wait(sp, s_rec, 2 * i + u - 1)
                        sp.dma_start(eas[:, u, :].rearrange("p (c d) -> p c d", d=ED),
                                     ea_e[:, bass.ds((2 * i + u) * CH, CH), :]).then_inc(s_ea[u], 16)
                load(0)
                with sp.Fori(1, EC // CH // 2) as i:
                    load(i)
                for u in range(2):
                    sp.wait_ge(s_placed[u], 16 * CH * (EC // CH // 2))
                def back(i):
                    for u in range(2):
                        wait(sp, s_meta, 2 * i + u - 1)
                        sp.dma_start(meta[:, u, :, :], rec_groups[bass.ds((2 * i + u) * 8, 8)].rearrange("g p w -> p g w")).then_inc(loaded[u], 16)
                back(0)
                if NG // 16 > 1:
                    with sp.Fori(1, NG // 16) as i:
                        back(i)
                if NG % 16:
                    sp.wait_ge(s_meta, NG // 8 - 2)
                    sp.dma_start(meta[:, 0, :, :], rec_groups[NG - 8:NG].rearrange("g p w -> p g w")).then_inc(loaded[0], 16)

            @block.gpsimd
            def _(pool):
                pool.memset(x[:, :, :], 0.0)
                pool.memset(blank[:, :, :], 0.0)
                pool.memset(ident[:, :], 0.0)
                pool.memset(ones[:, :], 1.0)
                pool.memset(tri[:, :], 1.0).then_inc(chain, 1)
                pool.wait_ge(chain, 1)
                pool.memset(blank[:, :, 2:3], -1.0)
                pool.affine_select(ident[:, :], ident[:, :], [[-1, P]], ALU.not_equal, 1.0, base=0, channel_multiplier=1)
                pool.affine_select(tri[:, :], tri[:, :], [[1, P]], ALU.is_gt, 0.0, base=0, channel_multiplier=-1)
                pool.iota(iota_row[:, :], [[1, P]], base=0, channel_multiplier=0, allow_small_or_imprecise_dtypes=True)
                pool.iota(iota_col[:, :], [[0, 1]], base=0, channel_multiplier=1, allow_small_or_imprecise_dtypes=True)
                pool.iota(kcol[:, :], [[1, BLOCKS]], base=0, channel_multiplier=0, allow_small_or_imprecise_dtypes=True)
                pool.memset(src_slot[:, NG * TILES:], 0.0)
                pool.memset(hwr_slot[:, NG * TILES:], 0.0)
                pool.memset(dst_slot16[:, NG * TILES:], -1.0)
                pool.iota(grow[:, :], [[1, NG]], base=0, channel_multiplier=0, allow_small_or_imprecise_dtypes=True).then_inc(go, 1)
                def place(i):
                    for u in range(2):
                        hold(pool, s_rec, 2 * i + u + 1)
                        for c in range(CH):
                            pool.indirect_dma_start(rec, bass.IndirectOffsetOnAxis(ap=posi[:, u, c:c + 1], axis=0),
                                                    reci[:, u, c, :], None).then_inc(s_placed[u], 16)
                pool.wait_ge(s_blank, 16 * (NG // 8))
                place(0)
                with pool.Fori(1, EC // CH // 2) as i:
                    place(i)

            @block.vector
            def _(dve):
                n = [1]

                def link(ins):
                    n[0] += 1
                    ins.then_inc(chain, 1)
                    dve.wait_ge(chain, n[0])

                dve.wait_ge(go, 1)
                dve.wait_ge(chain, 1)
                dve.tensor_copy(ident16[:, :], ident[:, :])
                dve.wait_ge(s_in, 16 * 5)
                link(dve.tensor_scalar(eq_i[:, :], dst_i[:, :], 7, None, ALU.arith_shift_right))
                link(dve.tensor_copy(blk[:, :], eq_i[:, :]))
                link(dve.tensor_scalar(eq_i[:, :], dst_i[:, :], P - 1, None, ALU.bitwise_and))
                link(dve.tensor_copy(loc[:, :], eq_i[:, :]))
                link(dve.tensor_copy(srcf[:, :], src_i[:, :]))
                link(dve.tensor_copy(hwr[:, :], et_i[:, :]))
                link(dve.scalar_tensor_tensor(hwr[:, :], hwr[:, :], float(NP), srcf[:, :], ALU.mult, ALU.add))
                link(dve.memset(pos[:, :], 0.0))

                def rank(k):
                    hold(dve, s_rank, k)
                    dve.tensor_scalar(eq[:, :], blk[:, :], kcol[0:EP, bass.ds(k, 1)], None, ALU.is_equal).then_inc(s_eq, 1)
                    wait(dve, s_eq, k + 1)
                    dve.tensor_tensor_scan(cum[:, :], eq[:, :], eq[:, :], 0.0, ALU.add, ALU.max).then_inc(s_cum, 1)
                    hold(dve, s_cum, k + 1)
                    dve.tensor_copy(cnt[:, bass.ds(k, 1)], cum[:, EC - 1:EC])
                    dve.tensor_tensor(tmp[:, :], eq[:, :], cum[:, :], ALU.mult).then_inc(s_prod, 1)
                    hold(dve, s_prod, k + 1)
                    dve.tensor_tensor(pos[:, :], pos[:, :], tmp[:, :], ALU.add).then_inc(s_rank, 1)
                rank(0)
                with dve.Fori(1, BLOCKS) as k:
                    rank(k)
                dve.wait_ge(s_rank, BLOCKS)
                dve.drain().then_inc(s_cnt, 1)
                dve.wait_ge(s_pre, 1)
                link(dve.tensor_copy(toti[:, :], psum[0][:, 0:BLOCKS]))
                link(dve.tensor_scalar(ng[:, :], toti[:, :], float(GROUP - 1), None, ALU.add))
                link(dve.tensor_copy(toti[:, :], ng[:, :]))
                link(dve.tensor_scalar(toti[:, :], toti[:, :], GROUP.bit_length() - 1, None, ALU.arith_shift_right))
                link(dve.tensor_copy(ng[:, :], toti[:, :]))
                link(dve.tensor_tensor_scan(endg[:, :], ng[:, :], ng[:, :], 0.0, ALU.add, ALU.max))
                link(dve.tensor_tensor(basep[:, :], endg[:, :], ng[:, :], ALU.subtract))
                link(dve.tensor_scalar(basep[:, :], basep[:, :], float(GROUP), -1.0, ALU.mult, ALU.add))
                link(dve.tensor_tensor(basep[0:EP, :], basep[0:EP, :], psum[1][0:EP, 0:BLOCKS], ALU.add))

                def place(k):
                    hold(dve, s_rank, BLOCKS + k)
                    dve.tensor_scalar(tmp[:, :], blk[:, :], kcol[0:EP, bass.ds(k, 1)], basep[0:EP, bass.ds(k, 1)],
                                      ALU.is_equal, ALU.mult).then_inc(s_prod, 1)
                    hold(dve, s_prod, BLOCKS + k + 1)
                    dve.tensor_tensor(pos[:, :], pos[:, :], tmp[:, :], ALU.add).then_inc(s_rank, 1)
                place(0)
                with dve.Fori(1, BLOCKS) as k:
                    place(k)
                dve.wait_ge(s_rank, 2 * BLOCKS)
                dve.drain().then_inc(s_pos, 1)
                Q = NG // 4
                for q in range(4):
                    link(dve.tensor_tensor(ge[:, :, :], grow[:, q * Q:(q + 1) * Q].unsqueeze(2).to_broadcast([1, Q, BLOCKS]),
                                           endg[0:1, :].unsqueeze(1).to_broadcast([1, Q, BLOCKS]), ALU.is_ge))
                    link(dve.tensor_reduce(gbf[:, q * Q:(q + 1) * Q], ge[:, :, :], AX_X, ALU.add))
                link(dve.tensor_scalar(gbf[:, :], gbf[:, :], float(BLOCKS - 1), None, ALU.min))
                link(dve.tensor_copy(block_of[:, :], gbf[:, :]))

                def slots(i, us):
                    for u in us:
                        g = 2 * i + u
                        at = bass.ds(g * 8 * TILES, 8 * TILES)
                        v = meta[:, u, :, :].rearrange("p g (j w) -> p (g j) w", w=REC)
                        hold(dve, loaded[u], 16 * i + 16)
                        dve.tensor_copy(src_slot[:, at], v[:, :, 0])
                        dve.tensor_copy(hwr_slot[:, at], v[:, :, 1])
                        dve.tensor_copy(dst_slot[:, at], v[:, :, 2])
                        dve.tensor_copy(dst_slot16[:, at], v[:, :, 2]).then_inc(s_meta, 1)
                slots(0, (0, 1))
                if NG // 16 > 1:
                    with dve.Fori(1, NG // 16) as i:
                        slots(i, (0, 1))
                if NG % 16:
                    slots(NG // 16, (0,))
                chain_end[0] = n[0]

            @block.tensor
            def _(pe):
                pe.wait_ge(go, 1)
                pe.wait_ge(s_cnt, 1)
                pe.matmul(psum[0][:, 0:BLOCKS], ones[0:EP, :], cnt[:, :], start=True, stop=True)
                pe.matmul(psum[1][:, 0:BLOCKS], tri[0:EP, :], cnt[:, :], start=True, stop=True).then_inc(s_pre, 1)

            @block.scalar
            def _(act):
                act.wait_ge(s_pos, 1)

                def build(i):
                    for u in range(2):
                        at = bass.ds((2 * i + u) * CH, CH)
                        hold(act, s_placed[u], 16 * CH * i)
                        act.copy(reci[:, u, :, 0], srcf[:, at])
                        act.copy(reci[:, u, :, 1], hwr[:, at])
                        act.copy(reci[:, u, :, 2], loc[:, at])
                        act.copy(reci[:, u, :, 3], loc[:, at])
                        act.copy(posi[:, u, :], pos[:, at])
                        hold(act, s_ea[u], 16 * i + 16)
                        act.copy(reci[:, u, :, 4:REC], eas[:, u, :].rearrange("p (c d) -> p c d", d=ED)).then_inc(s_rec, 1)
                build(0)
                with act.Fori(1, EC // CH // 2) as i:
                    build(i)
        grown(go, 1)
        grown(loaded[0], 16 * (NG // 16 + (1 if NG % 16 else 0)))
        grown(loaded[1], 16 * (NG // 16))

        def row(vec):
            return vec.rearrange("(a d) -> a d", a=1)

        def everywhere(vec):
            return vec.partition_broadcast(P)

        HOPS = temp.shape[0] - 1
        LAYERS = len(gat) + HOPS
        w_rel_sb = sb("w_rel_sb", [H, RELS, H])
        wx = sb("wx", [H, LAYERS, W])
        wt = sb("wt", [H, 3, H])
        a2 = sb("a2", [H, 3, 2])
        w1ab = sb("w1ab", [H, 2, H])
        w1c = sb("w1c", [ED, H])
        w2x = sb("w2x", [H + 1, H])
        w3ab = sb("w3ab", [H, 2, H])
        w4_sb = sb("w4_sb", [H, H])
        b3_col = sb("b3_col", [H, 1])
        rows_sb = sb("rows_sb", [P, 7, H])
        temp_sb = sb("temp_sb", [P, HOPS + 1])
        attn_b_sb = sb("attn_b_sb", [P, 1])

        link_count = [0]

        def linker(eng):
            def link(ins):
                link_count[0] += 1
                ins.then_inc(chain, 1)
                eng.wait_ge(chain, base[chain.name] + link_count[0])
            return link

        def end_chain():
            grown(chain, link_count[0])
            link_count[0] = 0

        grown(chain, chain_end[0])
        with nc.Block() as block:
            @block.sync
            def _(sp):
                loads = [(w_rel_sb[:, :, :], w_rel.rearrange("r d f -> d r f")),
                         (w1ab[:, :, :], w1[0:2 * H, :].rearrange("(k d) f -> d k f", k=2)),
                         (w1c[:, :], w1[2 * H:, :]), (w2x[0:H, :], w2), (w2x[H:H + 1, :], row(b2)),
                         (w3ab[:, :, :], w3.rearrange("(k d) f -> d k f", k=2)), (w4_sb[:, :], w4),
                         (b3_col[:, :], b3.rearrange("(d a) -> d a", a=1)),
                         (temp_sb[:, :], everywhere(temp)), (attn_b_sb[:, :], everywhere(attn_b))]
                loads += [(rows_sb[:, n, :], everywhere(v)) for n, v in enumerate((b1, b4, gamma, beta, *(l[3] for l in gat)))]
                for k, (wk, a_s, a_d, _) in enumerate(gat):
                    loads += [(wx[:, k, 0:H], wk), (a2[:, k, 0:1], a_s.rearrange("(d a) -> d a", a=1)),
                              (a2[:, k, 1:2], a_d.rearrange("(d a) -> d a", a=1))]
                for k in range(3, LAYERS):
                    loads += [(wx[:, k, H + n:H + n + 1], attn_w[n * H:(n + 1) * H].rearrange("(d a) -> d a", a=1)) for n in range(2)]
                for to, of in loads:
                    sp.dma_start(to, of).then_inc(s_in, 16)
                sp.wait_ge(s_in, 16 * (5 + len(loads)))
                sp.sem_inc(s_tab, 16)

            @block.tensor
            def _(pe):
                pe.wait_ge(s_tab, 16)
                for k in range(3):
                    pe.transpose(psum[0][0:H, k * H:(k + 1) * H], wx[:, k, 0:H], ident[0:H, 0:H]).then_inc(s_row, 1)
                pe.wait_ge(s_mask, 1)
                for k in range(3):
                    pe.matmul(psum[1][0:H, 2 * k:2 * k + 2], wt[:, k, :], a2[:, k, :], start=True, stop=True).then_inc(s_row, 1)

            @block.vector
            def _(dve):
                dve.wait_ge(s_tab, 16)
                for k in range(3, LAYERS):
                    dve.tensor_copy(wx[:, k, 0:H], ident[0:H, 0:H])
                dve.memset(tab[:, :, :], 1.0)
                dve.wait_ge(s_row, 3)
                dve.tensor_copy(wt[:, :, :], psum[0][0:H, 0:3 * H].rearrange("p (k h) -> p k h", k=3)).then_inc(s_mask, 1)
                dve.wait_ge(s_row, 6)
                dve.tensor_copy(wx[:, 0:3, H:W], psum[1][0:H, 0:6].rearrange("p (k h) -> p k h", k=3)).then_inc(s_mask, 1)
        grown(s_row, 6)
        grown(s_mask, 2)
        grown(s_tab, 16)

        QB = 4
        STEPS = NB // QB
        xs = sb("xs", [P, QB, H])
        xT = sb("xT", [H, QB * P])
        p_staged = sem("nodes_staged")
        p_tr = sem("nodes_transposed")
        p_xT = sem("transposes_copied")
        p_mm = sem("products_done")
        p_sink = sem("products_copied")
        p_store = sem("products_stored")

        def turns(eng, n, body):
            body(0)
            with eng.Fori(1, n - 1) as i:
                body(i)
            body(n - 1)

        def there(n, most):
            return not isinstance(n, int) or 0 <= n < most

        def project(of, weights, cols, sink, after=None, store=None):
            wide = QB * cols > 512
            outs = [psum[2 + q][:, 0:cols] if wide else psum[2][:, q * cols:(q + 1) * cols] for q in range(QB)]
            with nc.Block() as block:
                @block.vector
                def _(dve):
                    def stage(s):
                        hold(dve, p_tr, s)
                        dve.tensor_copy(xs[:, :, :], of[:, bass.ds(s * QB, QB), :]).then_inc(p_staged, 1)

                    def step(s):
                        if there(s + 1, STEPS):
                            stage(s + 1)
                        if store:
                            hold(dve, p_store, 16 * QB * s)
                        hold(dve, p_mm, s + 1)
                        sink(dve, s).then_inc(p_sink, 1)
                    stage(0)
                    turns(dve, STEPS, step)
                    dve.wait_ge(p_sink, base[p_sink.name] + STEPS)
                    if after:
                        after(dve, linker(dve))

                @block.scalar
                def _(act):
                    def step(s):
                        hold(act, p_mm, s)
                        hold(act, p_tr, s + 1)
                        act.copy(xT[:, :], psum[0][0:H, :]).then_inc(p_xT, 1)
                    turns(act, STEPS, step)

                @block.tensor
                def _(pe):
                    def transposes(s):
                        hold(pe, p_xT, s)
                        hold(pe, p_staged, s + 1)
                        for q in range(QB):
                            ins = pe.transpose(psum[0][0:H, q * P:(q + 1) * P], xs[:, q, :], ident[:, :])
                        ins.then_inc(p_tr, 1)

                    def step(s):
                        if there(s + 1, STEPS):
                            transposes(s + 1)
                        hold(pe, p_sink, s)
                        hold(pe, p_xT, s + 1)
                        for q in range(QB):
                            ins = pe.matmul(outs[q], xT[:, q * P:(q + 1) * P], weights, start=True, stop=True)
                        ins.then_inc(p_mm, 1)
                    transposes(0)
                    turns(pe, STEPS, step)

                if store:
                    @block.sync
                    def _(sp):
                        turns(sp, STEPS, lambda s: store(sp, s))
                        sp.wait_ge(p_store, base[p_store.name] + 16 * QB * STEPS)
            for s in (p_staged, p_tr, p_xT, p_mm, p_sink):
                grown(s, STEPS)
            if store:
                grown(p_store, 16 * QB * STEPS)
            end_chain()

        def store_table():
            with nc.Block() as block:
                @block.sync
                def _(sp):
                    sp.dma_start(table_blocks, tab[:, :, :]).then_inc(s_tab, 16)
                    sp.wait_ge(s_tab, base[s_tab.name] + 16)
            grown(s_tab, 16)

        G = sb("G", [P, RING, TILES, W])
        ixs = sb("ixs", [P, RING, TILES], U32)
        dts = sb("dts", [P, 2, TILES], BF16)
        mask = sb("mask", [P, 2, GROUP], BF16)
        hot_t = sb("hot_t", [P, 2, GROUP])
        hot = sb("hot", [P, 2, TILES, P])
        junk = sb("junk", [P, GROUP])
        q = sb("q", [P, 2, 6])
        lam = sb("lam", [P, 2, 2])
        decay = sb("decay", [P, 2])
        ez = sb("ez", [P, 2, 4, TILES])
        ew = sb("ew", [P, 2, TILES])
        P_row, P_as, P_ed, P_acc = psum[0:2], psum[2:4], psum[4:6], psum[6:8]

        def block_at(eng, g):
            return eng.value_load(block_of[0:1, bass.ds(g, 1)], min_val=0, max_val=NB - 1)

        def stage_idx(act, i, u, slots):
            hold(act, gathered[u], 16 * TILES * i)
            act.copy(ixs[:, u, :], slots[:, bass.ds((RING * i + u) * TILES, TILES)]).then_inc(idx_staged, 1)

        def stage_dst(act, i, u):
            g = RING * i + u
            hold(act, s_row, g - 1)
            act.copy(dts[:, u % 2, :], dst_slot16[:, bass.ds(g * TILES, TILES)]).then_inc(s_dst, 1)

        def gather(pool, i, u, source, freed):
            g = RING * i + u
            hold(pool, freed, g - RING + 1)
            hold(pool, idx_staged, g + 1)
            for j in range(TILES):
                pool.indirect_dma_start(G[:, u, j, :], None, source, bass.IndirectOffsetOnAxis(ap=ixs[:, u, j:j + 1], axis=0)).then_inc(gathered[u], 16)

        def rows_of_dst(pe, i, u):
            g = RING * i + u
            hold(pe, s_dst, g + 1)
            hold(pe, s_mask, g - 1)
            for j in range(TILES):
                ins = pe.matmul(P_row[u % 2][:, j * P:(j + 1) * P], dts[:, u % 2, j:j + 1].to_broadcast([P, P]), ident16[:, :],
                                start=True, stop=True)
            ins.then_inc(s_row, 1)

        def scatter(pe, i, u, what, cols):
            g = RING * i + u
            hold(pe, s_acc, g - 1)
            hold(pe, s_hot, g + 1)
            for j in range(TILES):
                ins = pe.matmul(P_acc[u % 2][:, 0:cols], hot[:, u % 2, j, :], what(u)[:, j, 0:cols], start=(j == 0), stop=(j == TILES - 1))
            ins.then_inc(s_scat, 1)

        def onehot(dve, i, u):
            g = RING * i + u
            hold(dve, s_scat, g - 1)
            for j in range(TILES):
                ins = dve.tensor_scalar(hot[:, u % 2, j, :], iota_row[:, :], dst_slot[:, bass.ds(g * TILES + j, 1)], None, ALU.is_equal)
            ins.then_inc(s_hot, 1)

        def accumulate(dve, i, u, b, cols):
            g = RING * i + u
            hold(dve, s_scat, g + 1)
            hold(dve, s_acc, g)
            at = acc[:, bass.ds(b, 1), 0:cols].rearrange("p a w -> p (a w)")
            dve.tensor_tensor(at, at, P_acc[u % 2][:, 0:cols], ALU.add).then_inc(s_acc, 1)

        def ring(body):
            def turn(i):
                for u in range(RING):
                    body(i, u)
            return turn

        def off(i, u, d):
            return i + (u + d) // RING, (u + d) % RING

        def exists(i, u, d):
            i, u = off(i, u, d)
            return there(RING * i + u, NG) if isinstance(i, int) else True

        def edges_sum():
            with nc.Block() as block:
                @block.gpsimd
                def _(pool):
                    turns(pool, ITERS, ring(lambda i, u: gather(pool, i, u, hw_table, s_scat)))

                @block.scalar
                def _(act):
                    stage_idx(act, 0, 0, hwr_slot)
                    stage_idx(act, 0, 1, hwr_slot)

                    def step(i, u):
                        if exists(i, u, 2):
                            stage_idx(act, *off(i, u, 2), hwr_slot)
                    turns(act, ITERS, ring(step))

                @block.vector
                def _(dve):
                    dve.memset(acc[:, :, :], 0.0)

                    def step(i, u):
                        onehot(dve, i, u)
                        accumulate(dve, i, u, block_at(dve, RING * i + u), W)
                    turns(dve, ITERS, ring(step))

                @block.tensor
                def _(pe):
                    def step(i, u):
                        hold(pe, gathered[u], 16 * TILES * (i + 1))
                        scatter(pe, i, u, lambda v: G[:, v, :, :], W)
                    turns(pe, ITERS, ring(step))
            grown(idx_staged, NG)
            for u in range(RING):
                grown(gathered[u], 16 * TILES * ITERS)
            for s in (s_scat, s_acc, s_hot):
                grown(s, NG)

        mean = sb("mean", [P, NB])
        s_var = sem("variance_done")
        s_std = sem("deviation_done")

        def normed(dve, link, y, to):
            wide = [P, NB, H]
            sq = tab[:, :, 0:H]
            link(dve.tensor_reduce(mean[:, :], y, AX_X, ALU.add))
            link(dve.tensor_scalar(mean[:, :], mean[:, :], 1.0 / H, None, ALU.mult))
            link(dve.tensor_tensor(y, y, mean[:, :].unsqueeze(2).to_broadcast(wide), ALU.subtract))
            link(dve.tensor_tensor(sq, y, y, ALU.mult))
            link(dve.tensor_reduce(mean[:, :], sq, AX_X, ALU.add))
            dve.tensor_scalar(mean[:, :], mean[:, :], 1.0 / H, EPS_LN, ALU.mult, ALU.add).then_inc(s_var, 1)
            grown(s_std, 1)
            dve.wait_ge(s_std, base[s_std.name])
            link(dve.reciprocal(mean[:, :], mean[:, :]))
            link(dve.tensor_tensor(to, y, mean[:, :].unsqueeze(2).to_broadcast(wide), ALU.mult))

        def deviations(act, times):
            for _ in range(times):
                grown(s_var, 1)
                act.wait_ge(s_var, base[s_var.name])
                act.activation(mean[:, :], mean[:, :], ACT.Sqrt).then_inc(s_std, 1)

        def node_part(norms, body):
            with nc.Block() as block:
                @block.vector
                def _(dve):
                    body(dve, linker(dve))

                @block.scalar
                def _(act):
                    deviations(act, norms)
            end_chain()

        y = aux

        hws = sb("hws", [P, QB, RELS, W])

        def sink_hw(dve, s):
            for n in range(QB):
                ins = dve.tensor_copy(hws[:, n, :, 0:H], psum[2 + n][:, 0:RELS * H].rearrange("p (r f) -> p r f", r=RELS))
            return ins

        def store_hw(sp, s):
            hold(sp, p_sink, s + 1)
            for n in range(QB):
                sp.dma_start(hw_blocks[bass.ds(s * QB + n, 1)].rearrange("b p r w -> (b p) r w"), hws[:, n, :, :]).then_inc(p_store, 16)

        node_part(0, lambda dve, link: dve.memset(hws[:, :, :, :], 1.0))
        project(x, w_rel_sb[:, :, :].rearrange("d r f -> d (r f)"), RELS * H, sink_hw, store=store_hw)
        edges_sum()

        def finish_l0(dve, link):
            wide = [P, NB, H]
            link(dve.tensor_copy(deg[:, :], acc[:, :, W - 1]))
            link(dve.tensor_scalar(mean[:, :], deg[:, :], 1.0, None, ALU.max))
            link(dve.reciprocal(mean[:, :], mean[:, :]))
            link(dve.tensor_tensor(y[:, :, :], acc[:, :, 0:H], mean[:, :].unsqueeze(2).to_broadcast(wide), ALU.mult))
            link(dve.tensor_scalar(tab[:, :, 0:H], x[:, :, :], 0.2, None, ALU.mult))
            link(dve.scalar_tensor_tensor(y[:, :, :], y[:, :, :], 1.0 - 0.2, tab[:, :, 0:H], ALU.mult, ALU.add))
            link(dve.tensor_scalar(y[:, :, :], y[:, :, :], 0.0, None, ALU.max))
            link(dve.tensor_scalar(mean[:, :], deg[:, :], 0.0, None, ALU.is_equal))
            link(dve.tensor_tensor(tab[:, :, 0:H], x[:, :, :], y[:, :, :], ALU.subtract))
            link(dve.tensor_tensor(tab[:, :, 0:H], tab[:, :, 0:H], mean[:, :].unsqueeze(2).to_broadcast(wide), ALU.mult))
            link(dve.tensor_tensor(y[:, :, :], y[:, :, :], tab[:, :, 0:H], ALU.add))
            link(dve.tensor_tensor(y[:, :, :], y[:, :, :], x[:, :, :], ALU.add))
            normed(dve, link, y[:, :, :], x[:, :, :])

        node_part(1, finish_l0)

        def sink_pq(dve, s):
            v = psum[2][:, :].rearrange("p (n k f) -> p n k f", n=QB, k=2)
            dve.tensor_copy(tab[:, bass.ds(s * QB, QB), 0:H], v[:, :, 0, :])
            return dve.tensor_copy(aux[:, bass.ds(s * QB, QB), :], v[:, :, 1, :])

        def add_b1(dve, link):
            link(dve.tensor_tensor(aux[:, :, :], aux[:, :, :], rows_sb[:, 0, :].unsqueeze(1).to_broadcast([P, NB, H]), ALU.add))
            dve.memset(acc[:, :, :], 0.0)

        project(x, w1ab[:, :, :].rearrange("d k f -> d (k f)"), 2 * H, sink_pq, after=add_b1)
        store_table()

        rc = sb("rc", [P, RING, TILES, REC])
        eaT = sb("eaT", [ED, 2, GROUP])
        qs = sb("qs", [P, 2, H])
        pre = sb("pre", [P, 2, TILES, H])
        act_out = sb("act_out", [P, 2, TILES, H])
        s_ea_t = sem("attributes_transposed")
        s_eaT = sem("attributes_copied")
        s_qs = sem("target_part_staged")
        s_pre = sem("preactivation_done")
        s_y = sem("preactivation_summed")
        s_silu = sem("silu_done")

        def edges_mlp():
            P_eaT, P_pre = psum[2:4], psum[4:6]
            with nc.Block() as block:
                @block.sync
                def _(sp):
                    def step(i, u):
                        g = RING * i + u
                        hold(sp, s_ea_t, g - RING + 1)
                        sp.dma_start(rc[:, u, :, :].rearrange("p j w -> p (j w)"),
                                     rec_groups[bass.ds(g, 1)].rearrange("g p w -> (g p) w")).then_inc(loaded[u], 16)
                    turns(sp, ITERS, ring(step))

                @block.gpsimd
                def _(pool):
                    turns(pool, ITERS, ring(lambda i, u: gather(pool, i, u, table, s_y)))

                @block.scalar
                def _(act):
                    for u in range(2):
                        stage_idx(act, 0, u, src_slot)
                        stage_dst(act, 0, u)

                    def step(i, u):
                        g = RING * i + u
                        if exists(i, u, 2):
                            stage_idx(act, *off(i, u, 2), src_slot)
                            stage_dst(act, *off(i, u, 2))
                        b = block_at(act, g)
                        hold(act, s_pre, g - 1)
                        act.copy(qs[:, u % 2, :], aux[:, bass.ds(b, 1), :].rearrange("p a f -> p (a f)")).then_inc(s_qs, 1)
                        hold(act, s_ea_t, g + 1)
                        act.copy(eaT[:, u % 2, :], P_eaT[u % 2][0:ED, :]).then_inc(s_eaT, 1)
                        if exists(i, u, -1):
                            silu(*off(i, u, -1))

                    def silu(i, u):
                        g = RING * i + u
                        hold(act, s_scat, g - 1)
                        hold(act, s_y, g + 1)
                        act.activation(act_out[:, u % 2, :, :], pre[:, u % 2, :, :], ACT.Silu).then_inc(s_silu, 1)
                    turns(act, ITERS, ring(step))
                    silu(*off(ITERS - 1, RING - 1, 0))

                @block.vector
                def _(dve):
                    def target_onehot(i, u):
                        g = RING * i + u
                        hold(dve, s_pre, g - 1)
                        hold(dve, s_row, g + 1)
                        dve.tensor_scalar(hot_t[:, u % 2, :], P_row[u % 2][:, :], iota_col[:, :], None, ALU.is_equal).then_inc(s_mask, 1)

                    def step(i, u):
                        g = RING * i + u
                        onehot(dve, i, u)
                        if exists(i, u, 1):
                            target_onehot(*off(i, u, 1))
                        if exists(i, u, -2):
                            finish(*off(i, u, -2))
                        hold(dve, gathered[u], 16 * TILES * (i + 1))
                        hold(dve, s_silu, g - 1)
                        hold(dve, s_pre, g + 1)
                        dve.tensor_tensor(pre[:, u % 2, :, :], P_pre[u % 2][:, 0:TILES * H].rearrange("p (j f) -> p j f", j=TILES),
                                          G[:, u, :, 0:H], ALU.add).then_inc(s_y, 1)

                    def finish(i, u):
                        accumulate(dve, i, u, block_at(dve, RING * i + u), H)
                    target_onehot(0, 0)
                    turns(dve, ITERS, ring(step))
                    finish(*off(ITERS - 1, RING - 1, -1))
                    finish(*off(ITERS - 1, RING - 1, 0))

                @block.tensor
                def _(pe):
                    def transpose_ea(i, u):
                        g = RING * i + u
                        hold(pe, s_eaT, g - 1)
                        hold(pe, loaded[u], 16 * (i + 1))
                        for j in range(TILES):
                            ins = pe.transpose(P_eaT[u % 2][0:ED, j * P:(j + 1) * P], rc[:, u, j, 4:REC], ident[:, :])
                        ins.then_inc(s_ea_t, 1)

                    def preactivation(i, u):
                        g = RING * i + u
                        hold(pe, s_y, g - 1)
                        hold(pe, s_qs, g + 1)
                        hold(pe, s_eaT, g + 1)
                        hold(pe, s_mask, g + 1)
                        for j in range(TILES):
                            to = P_pre[u % 2][:, j * H:(j + 1) * H]
                            pe.matmul(to, eaT[:, u % 2, j * P:(j + 1) * P], w1c[:, :], start=True, stop=False)
                            ins = pe.matmul(to, hot_t[:, u % 2, j * P:(j + 1) * P], qs[:, u % 2, :], start=False, stop=True)
                        ins.then_inc(s_pre, 1)

                    def step(i, u):
                        if exists(i, u, 1):
                            transpose_ea(*off(i, u, 1))
                        preactivation(i, u)
                        if exists(i, u, 2):
                            rows_of_dst(pe, *off(i, u, 2))
                        if exists(i, u, -1):
                            sums(*off(i, u, -1))

                    def sums(i, u):
                        hold(pe, s_silu, RING * i + u + 1)
                        scatter(pe, i, u, lambda v: act_out[:, v % 2, :, :], H)
                    rows_of_dst(pe, 0, 0)
                    rows_of_dst(pe, 0, 1)
                    transpose_ea(0, 0)
                    turns(pe, ITERS, ring(step))
                    sums(*off(ITERS - 1, RING - 1, 0))
            for u in range(RING):
                grown(gathered[u], 16 * TILES * ITERS)
                grown(loaded[u], 16 * ITERS)
            for s in (idx_staged, s_dst, s_row, s_mask, s_ea_t, s_eaT, s_qs, s_pre, s_y, s_silu, s_hot, s_scat, s_acc):
                grown(s, NG)

        edges_mlp()

        st = sb("st", [P, QB, H + 1])
        aT = sb("aT", [H + 1, QB * P])
        gT = sb("gT", [H, QB * P])
        uT = sb("uT", [H, QB * P])
        p_gT = sem("sums_done")
        p_gTc = sem("sums_copied")
        p_u = sem("update_done")
        p_silu = sem("update_silu_done")

        def node_mlp():
            with nc.Block() as block:
                @block.vector
                def _(dve):
                    link = linker(dve)
                    link(dve.tensor_copy(acc[:, :, H:H + 1], deg[:, :].unsqueeze(2)))

                    def step(s):
                        at = bass.ds(s * QB, QB)
                        hold(dve, p_tr, s)
                        dve.tensor_copy(xs[:, :, :], x[:, at, :])
                        dve.tensor_copy(st[:, :, :], acc[:, at, 0:H + 1]).then_inc(p_staged, 1)
                        hold(dve, p_mm, s + 1)
                        dve.tensor_copy(aux[:, at, :], psum[4][:, 0:QB * H].rearrange("p (n f) -> p n f", n=QB)).then_inc(p_sink, 1)
                    turns(dve, STEPS, step)

                @block.scalar
                def _(act):
                    def step(s):
                        hold(act, p_mm, s)
                        hold(act, p_tr, s + 1)
                        act.copy(xT[:, :], psum[0][0:H, :])
                        act.copy(aT[:, :], psum[1][0:H + 1, :]).then_inc(p_xT, 1)
                        hold(act, p_gT, s + 1)
                        act.copy(gT[:, :], psum[2][0:H, :]).then_inc(p_gTc, 1)
                        hold(act, p_u, s + 1)
                        act.activation(uT[:, :], psum[3][0:H, :], ACT.Silu, bias=b3_col[:, :]).then_inc(p_silu, 1)
                    turns(act, STEPS, step)

                @block.tensor
                def _(pe):
                    def step(s):
                        hold(pe, p_staged, s + 1)
                        for n in range(QB):
                            pe.transpose(psum[0][0:H, n * P:(n + 1) * P], xs[:, n, :], ident[:, :])
                            ins = pe.transpose(psum[1][0:H + 1, n * P:(n + 1) * P], st[:, n, :], ident[:, :])
                        ins.then_inc(p_tr, 1)
                        hold(pe, p_xT, s + 1)
                        pe.matmul(psum[2][0:H, :], w2x[:, :], aT[:, :], start=True, stop=True).then_inc(p_gT, 1)
                        hold(pe, p_gTc, s + 1)
                        pe.matmul(psum[3][0:H, :], w3ab[:, 0, :], xT[:, :], start=True, stop=False)
                        pe.matmul(psum[3][0:H, :], w3ab[:, 1, :], gT[:, :], start=False, stop=True).then_inc(p_u, 1)
                        hold(pe, p_sink, s)
                        hold(pe, p_silu, s + 1)
                        for n in range(QB):
                            ins = pe.matmul(psum[4][:, n * H:(n + 1) * H], uT[:, n * P:(n + 1) * P], w4_sb[:, :], start=True, stop=True)
                        ins.then_inc(p_mm, 1)
                    turns(pe, STEPS, step)
            for s in (p_staged, p_tr, p_xT, p_mm, p_sink, p_gT, p_gTc, p_u, p_silu):
                grown(s, STEPS)
            end_chain()

        node_mlp()

        def over_nodes(n):
            return rows_sb[:, n, :].unsqueeze(1).to_broadcast([P, NB, H])

        def finish_l1(dve, link):
            link(dve.tensor_tensor(y[:, :, :], y[:, :, :], over_nodes(1), ALU.add))
            link(dve.tensor_tensor(y[:, :, :], y[:, :, :], x[:, :, :], ALU.add))
            normed(dve, link, y[:, :, :], y[:, :, :])
            link(dve.tensor_tensor(y[:, :, :], y[:, :, :], over_nodes(2), ALU.mult))
            link(dve.tensor_tensor(y[:, :, :], y[:, :, :], over_nodes(3), ALU.add))
            link(dve.tensor_tensor(y[:, :, :], y[:, :, :], x[:, :, :], ALU.add))
            normed(dve, link, y[:, :, :], x[:, :, :])

        node_part(2, finish_l1)

        feat = sb("feat", [P, NB, H])

        def edges_attention(slope):
            with nc.Block() as block:
                @block.gpsimd
                def _(pool):
                    turns(pool, ITERS, ring(lambda i, u: gather(pool, i, u, table, s_scat)))

                @block.scalar
                def _(act):
                    def target_onehot(i, u):
                        g = RING * i + u
                        hold(act, s_ed, g - 1)
                        hold(act, s_mask, g + 1)
                        act.activation(hot_t[:, u % 2, :], mask[:, u % 2, :], ACT.Copy, bias=1.0, scale=1.0 / BIG).then_inc(s_hot_t, 1)

                    def weights(i, u):
                        g = RING * i + u
                        hold(act, s_hot, g - 1)
                        hold(act, s_x, g + 1)
                        act.activation(ew[:, u % 2, :], ez[:, u % 2, 3, :], ACT.Exp).then_inc(s_w, 1)

                    def step(i, u):
                        g = RING * i + u
                        if exists(i, u, 2):
                            stage_idx(act, *off(i, u, 2), src_slot)
                            stage_dst(act, *off(i, u, 2))
                        hold(act, s_acc, g - 1)
                        hold(act, s_mu, g + 1)
                        act.activation(decay[:, u % 2:u % 2 + 1], q[:, u % 2, 5:6], ACT.Exp, bias=q[:, u % 2, 3:4], scale=-1.0).then_inc(s_decay, 1)
                        if exists(i, u, 1):
                            target_onehot(*off(i, u, 1))
                        if exists(i, u, -1):
                            weights(*off(i, u, -1))
                    for u in range(2):
                        stage_idx(act, 0, u, src_slot)
                        stage_dst(act, 0, u)
                    target_onehot(0, 0)
                    turns(act, ITERS, ring(step))
                    weights(*off(ITERS - 1, RING - 1, 0))

                @block.vector
                def _(dve):
                    def mask_rows(i, u):
                        g = RING * i + u
                        hold(dve, s_max, g - 1)
                        hold(dve, s_hot_t, g - 1)
                        hold(dve, s_row, g + 1)
                        dve.tensor_scalar(mask[:, u % 2, :], P_row[u % 2][:, :], iota_col[:, :], -BIG, ALU.not_equal, ALU.mult).then_inc(s_mask, 1)

                    def greatest(i, u):
                        g = RING * i + u
                        b = block_at(dve, g)
                        v = q[:, u % 2, :]
                        hold(dve, s_ed, g - 1)
                        hold(dve, s_decay, g - 1)
                        hold(dve, s_upd, g)
                        dve.tensor_copy(v[:, 0:2], state[:, bass.ds(b, 1), :].rearrange("p a s -> p (a s)")).then_inc(s_old, 1)
                        hold(dve, s_as, g + 1)
                        hold(dve, s_mask, g + 1)
                        hold(dve, s_old, g + 1)
                        dve.tensor_tensor_reduce(junk[:, :], P_as[u % 2][:, :], mask[:, u % 2, :], 1.0, v[:, 0:1], ALU.add, ALU.max,
                                                 v[:, 2:3]).then_inc(s_max, 1)
                        hold(dve, s_max, g + 1)
                        dve.tensor_scalar(lam[:, u % 2, :], v[:, 0:3:2], v[:, 1:2], None, ALU.add).then_inc(s_sum, 1)
                        dve.tensor_copy(state[:, bass.ds(b, 1), 0:1].rearrange("p a s -> p (a s)"), v[:, 2:3]).then_inc(s_upd, 1)
                        hold(dve, s_sum, g + 1)
                        dve.scalar_tensor_tensor(v[:, 3:6:2], lam[:, u % 2, :], slope, lam[:, u % 2, :], ALU.mult, ALU.max).then_inc(s_mu, 1)

                    def exponents(i, u):
                        g = RING * i + u
                        z = ez[:, u % 2, :, :]
                        ed = P_ed[u % 2][:, 0:2 * TILES].rearrange("p (j k) -> p j k", k=2)
                        hold(dve, s_w, g - 1)
                        hold(dve, gathered[u], 16 * TILES * (i + 1))
                        hold(dve, s_ed, g + 1)
                        dve.tensor_tensor(z[:, 0, :], G[:, u, :, H], ed[:, :, 0], ALU.add).then_inc(s_z, 1)
                        hold(dve, s_z, g + 1)
                        dve.scalar_tensor_tensor(z[:, 1, :], z[:, 0, :], slope, z[:, 0, :], ALU.mult, ALU.max).then_inc(s_l, 1)
                        hold(dve, s_l, 2 * g + 1)
                        dve.tensor_tensor(z[:, 2, :], z[:, 1, :], ed[:, :, 1], ALU.subtract).then_inc(s_l, 1)
                        hold(dve, s_l, 2 * g + 2)
                        dve.tensor_scalar(z[:, 3, :], z[:, 2, :], 0.0, None, ALU.min).then_inc(s_x, 1)

                    def weighted_onehot(i, u):
                        g = RING * i + u
                        hold(dve, s_scat, g - 1)
                        hold(dve, s_w, g + 1)
                        for j in range(TILES):
                            ins = dve.tensor_scalar(hot[:, u % 2, j, :], iota_row[:, :], dst_slot[:, bass.ds(g * TILES + j, 1)],
                                                    ew[:, u % 2, j:j + 1], ALU.is_equal, ALU.mult)
                        ins.then_inc(s_hot, 1)

                    def shrink_and_add(i, u):
                        g = RING * i + u
                        b = block_at(dve, g)
                        at = acc[:, bass.ds(b, 1), :].rearrange("p a w -> p (a w)")
                        hold(dve, s_decay, g + 1)
                        hold(dve, s_scat, g + 1)
                        hold(dve, s_acc, g)
                        dve.scalar_tensor_tensor(at, at, decay[:, u % 2:u % 2 + 1], P_acc[u % 2][:, 0:W], ALU.mult, ALU.add).then_inc(s_acc, 1)

                    def step(i, u):
                        greatest(i, u)
                        if exists(i, u, 1):
                            mask_rows(*off(i, u, 1))
                        if exists(i, u, -1):
                            exponents(*off(i, u, -1))
                        if exists(i, u, -2):
                            shrink_and_add(*off(i, u, -2))
                        if exists(i, u, -1):
                            weighted_onehot(*off(i, u, -1))
                    mask_rows(0, 0)
                    turns(dve, ITERS, ring(step))
                    last = off(ITERS - 1, RING - 1, 0)
                    exponents(*last)
                    shrink_and_add(*off(*last, -1))
                    weighted_onehot(*last)
                    shrink_and_add(*last)

                @block.tensor
                def _(pe):
                    def rows_of_scores(i, u):
                        g = RING * i + u
                        hold(pe, s_max, g - 1)
                        hold(pe, gathered[u], 16 * TILES * (i + 1))
                        for j in range(TILES):
                            ins = pe.matmul(P_as[u % 2][:, j * P:(j + 1) * P], G[:, u, j, H:H + 1].to_broadcast([P, P]), ident[:, :],
                                            start=True, stop=True)
                        ins.then_inc(s_as, 1)

                    def to_edges(i, u):
                        g = RING * i + u
                        hold(pe, s_x, g - 1)
                        hold(pe, s_hot_t, g + 1)
                        hold(pe, s_mu, g + 1)
                        for j in range(TILES):
                            ins = pe.matmul(P_ed[u % 2][:, 2 * j:2 * j + 2], hot_t[:, u % 2, j * P:(j + 1) * P], q[:, u % 2, 1:6:4],
                                            start=True, stop=True)
                        ins.then_inc(s_ed, 1)

                    def step(i, u):
                        to_edges(i, u)
                        if exists(i, u, 1):
                            rows_of_scores(*off(i, u, 1))
                        if exists(i, u, 2):
                            rows_of_dst(pe, *off(i, u, 2))
                        if exists(i, u, -1):
                            scatter(pe, *off(i, u, -1), lambda v: G[:, v, :, :], W)
                    rows_of_dst(pe, 0, 0)
                    rows_of_dst(pe, 0, 1)
                    rows_of_scores(0, 0)
                    turns(pe, ITERS, ring(step))
                    scatter(pe, *off(ITERS - 1, RING - 1, 0), lambda v: G[:, v, :, :], W)
            for u in range(RING):
                grown(gathered[u], 16 * TILES * ITERS)
            for s in (idx_staged, s_dst, s_row, s_mask, s_hot_t, s_as, s_old, s_max, s_sum, s_upd, s_mu, s_decay, s_ed, s_z,
                      s_x, s_w, s_hot, s_scat, s_acc):
                grown(s, NG)
            grown(s_l, 2 * NG)

        def sink_att(dve, s):
            v = psum[2][:, 0:QB * W].rearrange("p (n w) -> p n w", n=QB)
            at = bass.ds(s * QB, QB)
            dve.tensor_copy(tab[:, at, 0:H + 1], v[:, :, 0:H + 1])
            return dve.tensor_copy(state[:, at, 1:2], v[:, :, H + 1:W])

        wide = [P, NB, H]

        def start_gat(dve, link):
            dve.tensor_copy(state[:, :, 0:1], tab[:, :, H:H + 1])
            dve.tensor_copy(acc[:, :, :], tab[:, :, :])

        def start_hop(dve, link):
            dve.tensor_scalar(state[:, :, 1], state[:, :, 1], attn_b_sb[:, :], None, ALU.add)
            dve.memset(state[:, :, 0:1], -BIG)
            dve.memset(acc[:, :, :], 0.0)

        def softmax_mean(dve, link):
            link(dve.tensor_scalar(mean[:, :], acc[:, :, W - 1], 1e-16, None, ALU.add))
            link(dve.reciprocal(mean[:, :], mean[:, :]))
            link(dve.tensor_tensor(feat[:, :, :], acc[:, :, 0:H], mean[:, :].unsqueeze(2).to_broadcast(wide), ALU.mult))

        def finish_gat(k):
            def body(dve, link):
                softmax_mean(dve, link)
                link(dve.tensor_tensor(feat[:, :, :], feat[:, :, :], over_nodes(4 + k), ALU.add))
                if k < len(gat) - 1:
                    link(dve.tensor_scalar(feat[:, :, :], feat[:, :, :], 0.0, None, ALU.max))
                else:
                    link(dve.tensor_tensor(feat[:, :, :], feat[:, :, :], x[:, :, :], ALU.add))
                    normed(dve, link, feat[:, :, :], x[:, :, :])
                    link(dve.tensor_scalar(y[:, :, :], x[:, :, :], temp_sb[:, 0:1], None, ALU.mult))
            return body

        def finish_hop(k):
            def body(dve, link):
                softmax_mean(dve, link)
                link(dve.scalar_tensor_tensor(y[:, :, :], feat[:, :, :], temp_sb[:, k + 1:k + 2], y[:, :, :], ALU.mult, ALU.add))
                if k == HOPS - 1:
                    link(dve.tensor_tensor(y[:, :, :], y[:, :, :], x[:, :, :], ALU.add))
                    normed(dve, link, y[:, :, :], x[:, :, :])
            return body

        for k in range(LAYERS):
            is_gat = k < len(gat)
            first = k in (0, len(gat))
            project(x if first else feat, wx[:, k, :], W, sink_att, after=start_gat if is_gat else start_hop)
            store_table()
            edges_attention(0.2 if is_gat else 0.01)
            node_part(int(k in (len(gat) - 1, LAYERS - 1)), finish_gat(k) if is_gat else finish_hop(k - len(gat)))

        with nc.Block() as block:
            @block.sync
            def _(sp):
                full = N // P
                sp.dma_start(out[0:full * P, :].rearrange("(b p) f -> p b f", p=P), x[:, 0:full, :]).then_inc(s_out, 16)
                if N % P:
                    sp.dma_start(out[full * P:N, :], x[0:N % P, full, :]).then_inc(s_out, 16)
                sp.wait_ge(s_out, 16 * (2 if N % P else 1))


_GAT = ["L2_gnn_W1", "L2_gnn_a1s", "L2_gnn_a1d", "L2_gnn_b1", "L2_gnn_W2", "L2_gnn_a2s", "L2_gnn_a2d", "L2_gnn_b2",
        "L2_gnn_W3", "L2_gnn_a3s", "L2_gnn_a3d", "L2_gnn_b3"]
_INS = ["x", "src", "dst", "edge_attr_32", "edge_type_8", "L0_gnn_weight_r", "L1_gnn_w1", "L1_gnn_b1", "L1_gnn_w2",
        "L1_gnn_b2", "L1_gnn_w3", "L1_gnn_b3", "L1_gnn_w4", "L1_gnn_b4", "L1_gnn_gamma", "L1_gnn_beta", *_GAT,
        "L3_gnn_attn_w", "L3_gnn_attn_b", "L3_gnn_temp"]


def kernel(**inputs):
    import numpy as _np
    import concourse.bacc as _bacc
    from concourse import mybir as _mybir
    from concourse.bass_utils import run_bass_kernel_spmd as _run

    nc = _bacc.Bacc("TRN2", target_bir_lowering=False, num_devices=1)
    arrays, args = {}, {}
    for name in _INS:
        a = _np.ascontiguousarray(inputs[name])
        arrays[f"in_{name}"] = a
        args[name] = nc.dram_tensor(f"in_{name}", a.shape, _mybir.dt.from_np(a.dtype), kind="ExternalInput").ap()
    shape = inputs["x"].shape
    out = nc.dram_tensor("out_x", shape, _mybir.dt.float32, kind="ExternalOutput").ap()
    gat = [[args[n] for n in _GAT[4 * k:4 * k + 4]] for k in range(3)]
    a = [args[n] for n in _INS if n not in _GAT]
    gnn_kernel(nc, *a[:16], gat, *a[16:], out)
    r = _run(nc, [arrays], core_ids=[0])
    return r.results[0]["out_x"]
```
